# Optimizing a Trainium2 kernel written in Bass

```python
import numpy as np
import jax
import jax.numpy as jnp

def _softmax(x, axis=-1):
    return jax.nn.softmax(x, axis=axis)

def _gelu(x):
    return jax.nn.gelu(x, approximate=True)

def _silu(x):
    return jax.nn.silu(x)

def _sigmoid(x):
    return jax.nn.sigmoid(x)

def _layernorm(x, axis=-1, eps=1e-05):
    m = jnp.mean(x, axis=axis, keepdims=True)
    v = jnp.var(x, axis=axis, keepdims=True)
    return (x - m) / jnp.sqrt(v + eps)

def _scatter_add(tgt, idx, src, axis=0):
    return tgt.at[idx].add(src)

def _segment_sum(src, seg, n):
    return jax.ops.segment_sum(src, seg, n)
kernel_name = 'mk_gnn_preln_d2_gnn_r8_d22651'

def setup_inputs(seed: int=0):
    np.random.seed(seed)
    _w = jnp.asarray

    def _rec_inputs():
        import jax
        import jax.numpy as jnp
        _gk = jax.random.key(seed)
        x = -0.0005121 + 1.001 * jax.random.normal(jax.random.fold_in(_gk, 1), (6250, 64), jnp.float32)
        _s = jax.random.randint(jax.random.fold_in(_gk, 2), (100000,), 0, 6250, jnp.int32)
        _d = jax.random.randint(jax.random.fold_in(_gk, 3), (100000,), 0, 6250, jnp.int32)
        _loop = jnp.arange(6250, dtype=jnp.int32)
        src = jnp.concatenate([_s, _d, _loop])
        dst = jnp.concatenate([_d, _s, _loop])
        _o = jnp.argsort(dst, stable=True)
        src = src[_o]
        dst = dst[_o]
        edge_attr_16 = 0.000312547 + 1.00004 * jax.random.normal(jax.random.fold_in(_gk, 11), (206250, 16), jnp.float32)
        edge_attr_64 = -6.74381e-05 + 0.999835 * jax.random.normal(jax.random.fold_in(_gk, 12), (206250, 64), jnp.float32)
        return (x, src, dst, edge_attr_16, edge_attr_64)
    x, src, dst, edge_attr_16, edge_attr_64 = _rec_inputs()

    def _L0_gnn_setup():
        import jax, jax.numpy as jnp
        import numpy as np
        N_NODES = 6250
        N_EDGES = 125000
        IN_SIZE = 64
        OUT_SIZE = 64
        EDGE_DIM = 16
        BN_EPS = 1e-05
        GIN_EPS = 0.0
        key = jax.random.key(seed)
        ks = jax.random.split(key, 10)
        s = 1.0 / np.sqrt(IN_SIZE)
        return {'x': jax.random.normal(ks[0], (N_NODES, IN_SIZE), dtype=jnp.float32), 'edge_index': jax.random.randint(ks[1], (2, N_EDGES), 0, N_NODES, dtype=jnp.int64), 'edge_attr': jax.random.normal(ks[2], (N_EDGES, EDGE_DIM), dtype=jnp.float32), 'W_edge': jax.random.uniform(ks[3], (IN_SIZE, EDGE_DIM), jnp.float32, -s, s), 'b_edge': jnp.zeros((IN_SIZE,), jnp.float32), 'W1': jax.random.uniform(ks[4], (OUT_SIZE, IN_SIZE), jnp.float32, -s, s), 'b1': jnp.zeros((OUT_SIZE,), jnp.float32), 'gamma': jnp.ones((OUT_SIZE,), jnp.float32), 'beta': jnp.zeros((OUT_SIZE,), jnp.float32), 'W2': jax.random.uniform(ks[5], (OUT_SIZE, OUT_SIZE), jnp.float32, -1.0 / np.sqrt(OUT_SIZE), 1.0 / np.sqrt(OUT_SIZE)), 'b2': jnp.zeros((OUT_SIZE,), jnp.float32)}
    _L0_gnn_all = _L0_gnn_setup()
    _L0_gnn_in = {k: v for k, v in _L0_gnn_all.items() if k in ('W_edge', 'b_edge', 'W1', 'b1', 'gamma', 'beta', 'W2', 'b2')}
    del _L0_gnn_all

    def _L1_gnn_setup():
        import jax, jax.numpy as jnp
        import numpy as np
        N_NODES = 6250
        N_EDGES = 156250
        D_NODE = 64
        D_EDGE = 64
        M_OUT = 64
        U_OUT = 64
        key = jax.random.key(seed)
        k1, k2, k3, k4, k5, k6 = jax.random.split(key, 6)
        H = jax.random.normal(k1, (N_NODES, D_NODE), dtype=jnp.float32)
        Xe = jax.random.normal(k2, (N_EDGES, D_EDGE), dtype=jnp.float32)
        id_Xe = jax.random.randint(k3, (2, N_EDGES), 0, N_NODES, dtype=jnp.int64)
        M_W = jax.random.normal(k4, (M_OUT, D_NODE + D_EDGE), dtype=jnp.float32) * 0.05
        M_b = jnp.zeros((M_OUT,), dtype=jnp.float32)
        U_W = jax.random.normal(k5, (U_OUT, D_NODE + M_OUT), dtype=jnp.float32) * 0.05
        U_b = jnp.zeros((U_OUT,), dtype=jnp.float32)
        return {'H': H, 'Xe': Xe, 'id_Xe': id_Xe, 'M_W': M_W, 'M_b': M_b, 'U_W': U_W, 'U_b': U_b}
    _L1_gnn_all = _L1_gnn_setup()
    _L1_gnn_in = {k: v for k, v in _L1_gnn_all.items() if k in ('M_W', 'M_b', 'U_W', 'U_b')}
    del _L1_gnn_all
    return {'x': x, 'src': src, 'dst': dst, 'edge_attr_16': edge_attr_16, 'edge_attr_64': edge_attr_64, 'L0_gnn_W_edge': _L0_gnn_in['W_edge'], 'L0_gnn_b_edge': _L0_gnn_in['b_edge'], 'L0_gnn_W1': _L0_gnn_in['W1'], 'L0_gnn_b1': _L0_gnn_in['b1'], 'L0_gnn_gamma': _L0_gnn_in['gamma'], 'L0_gnn_beta': _L0_gnn_in['beta'], 'L0_gnn_W2': _L0_gnn_in['W2'], 'L0_gnn_b2': _L0_gnn_in['b2'], 'L1_gnn_M_W': _L1_gnn_in['M_W'], 'L1_gnn_M_b': _L1_gnn_in['M_b'], 'L1_gnn_U_W': _L1_gnn_in['U_W'], 'L1_gnn_U_b': _L1_gnn_in['U_b']}

def reference(x, src, dst, edge_attr_16, edge_attr_64, L0_gnn_W_edge, L0_gnn_b_edge, L0_gnn_W1, L0_gnn_b1, L0_gnn_gamma, L0_gnn_beta, L0_gnn_W2, L0_gnn_b2, L1_gnn_M_W, L1_gnn_M_b, L1_gnn_U_W, L1_gnn_U_b):
    import jax
    import jax.numpy as jnp

    def _L0_gnn_ref(x, edge_index, edge_attr, W_edge, b_edge, W1, b1, gamma, beta, W2, b2):
        import jax, jax.numpy as jnp
        import numpy as np
        N_NODES = 6250
        N_EDGES = 125000
        IN_SIZE = 64
        OUT_SIZE = 64
        EDGE_DIM = 16
        BN_EPS = 1e-05
        GIN_EPS = 0.0
        src = edge_index[0]
        dst = edge_index[1]
        ea = edge_attr @ W_edge.T + b_edge
        msg = jax.nn.relu(x[src] + ea)
        agg = jax.ops.segment_sum(msg, dst, num_segments=x.shape[0])
        h = (1.0 + GIN_EPS) * x + agg
        h = h @ W1.T + b1
        mean = jnp.mean(h, axis=0)
        var = jnp.var(h, axis=0)
        h = gamma * (h - mean) * jax.lax.rsqrt(var + BN_EPS) + beta
        h = jax.nn.relu(h)
        return h @ W2.T + b2

    def _L1_gnn_ref(H, Xe, id_Xe, M_W, M_b, U_W, U_b):
        import jax, jax.numpy as jnp
        import numpy as np
        N_NODES = 6250
        N_EDGES = 156250
        D_NODE = 64
        D_EDGE = 64
        M_OUT = 64
        U_OUT = 64
        features = H[id_Xe[0]]
        M_in = jnp.concatenate([features, Xe], axis=1)
        Y = jax.nn.relu(M_in @ M_W.T + M_b)
        Z = jax.ops.segment_sum(Y, id_Xe[1], num_segments=H.shape[0])
        U_in = jnp.concatenate([H, Z], axis=1)
        H_next = jax.nn.relu(U_in @ U_W.T + U_b)
        return H_next
    edge_index = jnp.stack([src, dst])
    h = jnp.maximum(_layernorm(x, axis=-1), 0.0)
    x = x + _L0_gnn_ref(h, edge_index, edge_attr_16, L0_gnn_W_edge, L0_gnn_b_edge, L0_gnn_W1, L0_gnn_b1, L0_gnn_gamma, L0_gnn_beta, L0_gnn_W2, L0_gnn_b2)
    h = jnp.maximum(_layernorm(x, axis=-1), 0.0)
    x = x + _L1_gnn_ref(h, edge_attr_64, edge_index, L1_gnn_M_W, L1_gnn_M_b, L1_gnn_U_W, L1_gnn_U_b)
    return x

_drawn_inputs = setup_inputs


def setup_inputs(seed=0):
    import zlib

    import numpy as np

    out = dict(_drawn_inputs(seed))
    spreads = {'L0_gnn_b_edge': (0.0, 0.417),
     'L0_gnn_b1': (0.0, 0.8),
     'L0_gnn_gamma': (1.0, 0.2),
     'L0_gnn_beta': (0.0, 0.329),
     'L0_gnn_b2': (0.0, 0.1),
     'L1_gnn_M_b': (0.0, 0.1),
     'L1_gnn_U_b': (0.0, 0.1)}
    factors = {}
    for name, (base, spread) in spreads.items():
        noise = np.random.default_rng([zlib.crc32(name.encode()), seed]).standard_normal(out[name].shape)
        drawn = base * np.exp(spread * noise) if base else spread * noise
        out[name] = jnp.asarray(drawn.astype(out[name].dtype))
    for name, factor in factors.items():
        out[name] = (out[name] * factor).astype(out[name].dtype)
    return out
```

```python
from contextlib import ExitStack

import numpy as np

import concourse.bass as bass
from concourse import mybir

F32 = mybir.dt.float32
I32 = mybir.dt.int32
ALU = mybir.AluOpType
ACT = mybir.ActivationFunctionType
AX_X = mybir.AxisListType.X

N = 6250
D = 64
EDGES = 206250
EDGE_DIM = (16, 64)
NODE_P = 125
NODE_COLS = N // NODE_P
P = 128
BATCH = 13
TILES = 1612
BATCHES = TILES // BATCH
PAIRS = BATCHES // 2
WINDOW = 64
PASSES = -(-N // WINDOW)
AGG_COLS = N + WINDOW + 6
GROUP = 8
GROUPS = [(j, min(GROUP, NODE_COLS - j)) for j in range(0, NODE_COLS, GROUP)]
NG = len(GROUPS)
Z_CHUNK = 500
Z_CHUNKS = [(c, min(Z_CHUNK, N - c)) for c in range(0, N, Z_CHUNK)]
STAT_CHUNK = 250
LN_EPS = 1e-5
BN_EPS = 1e-5

assert NODE_P * NODE_COLS == N and TILES * P >= EDGES and BATCHES * BATCH == TILES and BATCHES % 2 == 0
assert BATCHES <= P

PARAMS = {}
PARAM_COLS = 0
for _name, _width in (("identity", P), ("iota", WINDOW), ("ones", P), ("w_edge", D), ("b_edge", D), ("w1", D),
                      ("w2", D), ("m_node", D), ("m_edge", D), ("u_node", D), ("u_sum", D),
                      ("b1", 1), ("gamma", 1), ("beta", 1), ("eps", 1)):
    PARAMS[_name] = slice(PARAM_COLS, PARAM_COLS + _width)
    PARAM_COLS += _width


class EdgeSems:

    def __init__(self, sem, layer):
        def pair(what):
            return [sem(f"{what}_l{layer}_s{s}") for s in range(2)]

        self.idx_ready = pair("idx_ready")
        self.gathers_begun = sem(f"gathers_begun_l{layer}")
        self.pass_begun = sem(f"pass_begun_l{layer}")
        self.rows_landed = pair("rows_landed")
        self.attr_landed = pair("attr_landed")
        self.projected = pair("projected")
        self.added = pair("added")
        self.relu_done = pair("relu_done")
        self.onehot_done = pair("onehot_done")
        self.scattered = pair("scattered")
        self.accumulated = pair("accumulated")


def done(k):
    return k + 2


def freed(k):
    return k + 1


def build(nc, x, idx, dst, attr0, attr1, params, out):
    attrs = (attr0, attr1)
    table = [nc.dram_tensor(f"node_table_l{layer}", (N, D), F32, kind="Internal").ap() for layer in range(2)]
    with ExitStack() as ctx:
        def sb(name, shape, dt=F32):
            return ctx.enter_context(nc.sbuf_tensor(name, shape, dt))

        def ps(name, shape):
            return ctx.enter_context(nc.psum_tensor(name, shape, F32))

        def sem(name):
            return ctx.enter_context(nc.semaphore(name))

        par = sb("par", [P, PARAM_COLS])
        idx_all = sb("idx_all", [P, TILES + 2 * BATCH], I32)
        dst_int = sb("dst_int", [P, TILES], I32)
        rel = sb("rel", [P, TILES])
        idx_slot = sb("idx_slot", [P, 2, BATCH], I32)
        rows = sb("rows", [P, 2, BATCH * D])
        attr_buf = sb("attr_buf", [D, 2, BATCH * P])
        pre = sb("pre", [P, 2, BATCH * D])
        msg = sb("msg", [P, 2, BATCH * D])
        onehot = sb("onehot", [P, 2, BATCH, WINDOW])
        agg = sb("agg", [D, AGG_COLS])
        zT = sb("zT", [D, N])
        hT = sb("hT", [D + 1, NODE_COLS, NODE_P])
        xs = sb("xs", [NODE_P, NODE_COLS, D])
        xc = sb("xc", [NODE_P, NODE_COLS, D])
        sq = sb("sq", [NODE_P, NODE_COLS, D])
        ln_sum = sb("ln_sum", [NODE_P, NODE_COLS])
        ln_var = sb("ln_var", [NODE_P, NODE_COLS])
        ln_std = sb("ln_std", [NODE_P, NODE_COLS])
        ln_inv = sb("ln_inv", [NODE_P, NODE_COLS])
        ext = sb("ext", [P, 2, BATCHES])
        lohi = sb("lohi", [P, 4])
        base_row = sb("base_row", [1, BATCHES])
        base_int = sb("base_int", [1, BATCHES], I32)
        flags = sb("flags", [1, 4])
        flag_int = sb("flag_int", [1, 1], I32)
        bn = sb("bn", [D, N // STAT_CHUNK, nc.vector.BN_STATS_DIM])
        bn_mv = sb("bn_mv", [D, nc.vector.BN_AGGR_DIM])
        bn_t = sb("bn_t", [D, 6])

        ps_edge = [ps(f"ps_edge{s}", [P, 1024]) for s in range(2)]
        ps_win = [ps(f"ps_win{s}", [P, 512]) for s in range(2)]
        ps_node = [ps(f"ps_node{s}", [P, 512]) for s in range(2)]

        agg_nodes = agg[:, 0:N].rearrange("f (p j) -> f j p", j=NODE_COLS)
        z_nodes = zT[:, :].rearrange("f (p j) -> f j p", j=NODE_COLS)

        def prm(name, rows_n=P):
            return par[0:rows_n, PARAMS[name]]

        par_landed = sem("par_landed")
        x_landed = sem("x_landed")
        dst_landed = sem("dst_landed")
        idx_landed = sem("idx_landed")
        range_v = sem("range_v")
        range_t = sem("range_t")
        windows_set = sem("windows_set")
        windows_ready = sem("windows_ready")

        def per_layer(what):
            return [sem(f"{what}_l{layer}") for layer in range(2)]

        summed = per_layer("summed")
        centred = per_layer("centred")
        squared = per_layer("squared")
        var_done = per_layer("var_done")
        std_done = per_layer("std_done")
        inv_done = per_layer("inv_done")
        normed = per_layer("normed")
        turned = per_layer("turned")
        turn_copied = per_layer("turn_copied")
        rows_ready = per_layer("rows_ready")
        table_stored = per_layer("table_stored")
        sums_ready = per_layer("sums_ready")
        sums_done = per_layer("sums_done")
        pass_set = per_layer("pass_set")
        ones_set = sem("ones_set")
        z_done = sem("z_done")
        z_copied = sem("z_copied")
        bn_stat = sem("bn_stat")
        bn_v = sem("bn_v")
        bn_std = sem("bn_std")
        bn_h = sem("bn_h")
        w2_done = sem("w2_done")
        x1_done = sem("x1_done")
        table_mm = sem("table_mm")
        u_done = sem("u_done")
        result_ready = sem("result_ready")
        out_stored = sem("out_stored")
        edge_sems = [EdgeSems(sem, layer) for layer in range(2)]

        block = ctx.enter_context(nc.Block())

        def edge_passes(eng, one_pair, first_step=None, last_step=None):
            with eng.Fori(0, PAIRS) as k:
                one_pair(k, k)
            eng.wait_ge(windows_ready, 1)
            more = eng.value_load(flag_int[0:1, 0:1], min_val=0, max_val=1)
            with eng.If(more > 0):
                with eng.Fori(1, PASSES) as q:
                    if first_step is not None:
                        first_step(q)
                    with eng.Fori(0, PAIRS) as k:
                        one_pair(k, q * PAIRS + k)
                if last_step is not None:
                    last_step()
                eng.nop()
            with eng.Else():
                eng.nop()
            eng.nop()

        @block.sync
        def _(sp):
            for j, m in GROUPS:
                sp.dma_start(xs[:, j:j + m, :], x[:, j:j + m, :]).then_inc(x_landed, 16)
            sp.dma_start(par[:, :], params).then_inc(par_landed, 16)
            sp.dma_start(dst_int[:, :], dst).then_inc(dst_landed, 16)
            sp.dma_start(idx_all[:, :], idx).then_inc(idx_landed, 16)
            for layer in range(2):
                e, kd = edge_sems[layer], EDGE_DIM[layer]
                rows_of = table[layer].rearrange("(p j) d -> p j d", j=NODE_COLS)
                for g, (j, m) in enumerate(GROUPS):
                    sp.wait_ge(rows_ready[layer], g + 1)
                    sp.dma_start(rows_of[:, j:j + m, :], sq[:, j:j + m, :]).then_inc(table_stored[layer], 16)

                def one_pair(k, n):
                    for s in range(2):
                        sp.wait_ge(e.projected[s], freed(n))
                        sp.dma_start(attr_buf[0:kd, s, :],
                                     attrs[layer][bass.ds(k * 2 + s, 1)].rearrange("a d e -> (a d) e"))\
                            .then_inc(e.attr_landed[s], 16)

                edge_passes(sp, one_pair)
            for g, (j, m) in enumerate(GROUPS):
                sp.wait_ge(result_ready, g + 1)
                sp.dma_start(out[:, j:j + m, :], xc[:, j:j + m, :]).then_inc(out_stored, 16)
            sp.wait_ge(out_stored, 16 * NG)

        @block.gpsimd
        def _(pool):
            pool.memset(hT[D:D + 1, :, :], 1.0).then_inc(ones_set, 1)
            pool.wait_ge(ones_set, 1)
            pool.memset(agg[:, N:AGG_COLS], 0.0).then_inc(sums_ready[0], 1)
            pool.wait_ge(sums_ready[0], 1)
            pool.wait_ge(par_landed, 16)
            for g, (j, m) in enumerate(GROUPS):
                pool.wait_ge(normed[0], g + 1)
                pool.tensor_tensor(sq[:, j:j + m, :], xc[:, j:j + m, :],
                                   prm("b_edge", NODE_P).unsqueeze(1).broadcast_to([NODE_P, m, D]), ALU.add)\
                    .then_inc(rows_ready[0], 1)
            for layer in range(2):
                e = edge_sems[layer]
                if layer == 1:
                    pool.wait_ge(z_done, len(Z_CHUNKS))
                    pool.wait_ge(rows_ready[0], NG)
                    pool.memset(agg[:, :], 0.0).then_inc(sums_ready[1], 1)

                def one_pair(k, n):
                    for s in range(2):
                        pool.wait_ge(e.idx_ready[s], n + 1)
                        pool.wait_ge(e.added[s], freed(n))
                        pool.sem_inc(e.gathers_begun, 1)
                        for t in range(BATCH):
                            pool.indirect_dma_start(
                                out=rows[:, s, t * D:(t + 1) * D], out_offset=None, in_=table[layer],
                                in_offset=bass.IndirectOffsetOnAxis(ap=idx_slot[:, s, t:t + 1], axis=0),
                            ).then_inc(e.rows_landed[s], 16)

                pool.wait_ge(table_stored[layer], 16 * NG)
                edge_passes(pool, one_pair)

        @block.scalar
        def _(act):
            for e in edge_sems:
                for s in range(2):
                    act.sem_inc(e.relu_done[s], 1)
            act.wait_ge(par_landed, 16)

            def norm_roots(layer):
                for g, (j, m) in enumerate(GROUPS):
                    act.wait_ge(centred[layer], g + 1)
                    act.activation(sq[:, j:j + m, :], xc[:, j:j + m, :], ACT.Square).then_inc(squared[layer], 1)
                for g, (j, m) in enumerate(GROUPS):
                    act.wait_ge(var_done[layer], g + 1)
                    act.activation(ln_std[:, j:j + m], ln_var[:, j:j + m], ACT.Sqrt,
                                   bias=prm("eps", NODE_P), scale=1.0 / D).then_inc(std_done[layer], 1)

            def copy_turned(layer, to):
                for g, (j, m) in enumerate(GROUPS):
                    act.wait_ge(turned[layer], g + 1)
                    act.activation(to[:, j:j + m, :],
                                   ps_edge[g % 2][0:D, :].rearrange("f (j p) -> f j p", p=P)[:, 0:m, 0:NODE_P],
                                   ACT.Copy).then_inc(turn_copied[layer], 1)

            def edges(layer):
                e = edge_sems[layer]

                def one_pair(k, n):
                    for s in range(2):
                        act.wait_ge(e.added[s], done(n))
                        act.wait_ge(e.scattered[s], freed(n))
                        act.activation(msg[:, s, :], pre[:, s, :], ACT.Relu).then_inc(e.relu_done[s], 1)

                edge_passes(act, one_pair)

            norm_roots(0)
            copy_turned(0, agg_nodes)
            edges(0)
            for c, (a, w) in enumerate(Z_CHUNKS):
                act.wait_ge(z_done, c + 1)
                act.activation(zT[:, a:a + w], ps_node[c % 2][0:D, 0:w], ACT.Identity, bias=prm("b1", D))\
                    .then_inc(z_copied, 1)
            act.wait_ge(bn_v, 1)
            act.activation(bn_t[:, 0:1], bn_mv[:, 1:2], ACT.Sqrt, bias=prm("eps", D)).then_inc(bn_std, 1)
            act.wait_ge(bn_v, 5)
            act.wait_ge(z_copied, len(Z_CHUNKS))
            for g, (j, m) in enumerate(GROUPS):
                act.activation(hT[0:D, j:j + m, :], z_nodes[:, j:j + m, :], ACT.Relu,
                               scale=bn_t[:, 2:3], bias=bn_t[:, 4:5]).then_inc(bn_h, 1)
            act.wait_ge(table_stored[0], 16 * NG)
            norm_roots(1)
            act.wait_ge(w2_done, NG)
            copy_turned(1, hT[0:D, :, :])
            edges(1)

        @block.tensor
        def _(pe):
            for e in edge_sems:
                for s in range(2):
                    pe.sem_inc(e.projected[s], 1)
                    pe.sem_inc(e.scattered[s], 1)
            pe.wait_ge(par_landed, 16)

            def turn(layer):
                for g, (j, m) in enumerate(GROUPS):
                    pe.wait_ge(normed[layer], g + 1)
                    if g >= 2:
                        pe.wait_ge(turn_copied[layer], g - 1)
                    for i in range(m):
                        last = pe.transpose(ps_edge[g % 2][0:D, i * P:i * P + NODE_P], xc[:, j + i, :],
                                            prm("identity", NODE_P)[:, 0:NODE_P])
                    last.then_inc(turned[layer], 1)

            def edges(layer):
                e, kd = edge_sems[layer], EDGE_DIM[layer]
                weights = prm(("w_edge", "m_edge")[layer], kd)

                def one_pair(k, n):
                    for s in range(2):
                        pe.wait_ge(e.attr_landed[s], (n + 1) * 16)
                        pe.wait_ge(e.added[s], freed(n))
                        for t in range(BATCH):
                            last = pe.matmul(ps_edge[s][:, t * D:(t + 1) * D],
                                             attr_buf[0:kd, s, t * P:(t + 1) * P], weights,
                                             start=True, stop=True)
                        last.then_inc(e.projected[s], 1)
                        pe.wait_ge(e.relu_done[s], done(n))
                        pe.wait_ge(e.onehot_done[s], n + 1)
                        pe.wait_ge(e.accumulated[s], freed(n))
                        for t in range(BATCH):
                            last = pe.matmul(ps_win[s][0:D, 0:WINDOW], msg[:, s, t * D:(t + 1) * D],
                                             onehot[:, s, t, :], start=(t == 0), stop=(t == BATCH - 1))
                        last.then_inc(e.scattered[s], 1)

                edge_passes(pe, one_pair)

            pe.wait_ge(range_v, 3)
            for i in range(2):
                last = pe.transpose(ps_node[0][0:BATCHES, P * i:P * i + P], ext[:, i, :], prm("identity"))
            last.then_inc(range_t, 1)
            pe.wait_ge(range_v, 6)
            for i in range(2):
                last = pe.transpose(ps_node[1][0:1, P * i:P * i + BATCHES], lohi[0:BATCHES, 2 * i:2 * i + 1],
                                    prm("identity", BATCHES)[:, 0:BATCHES])
            last.then_inc(range_t, 1)
            pe.wait_ge(range_v, 10)
            pe.matmul(ps_node[0][:, 0:BATCHES], prm("ones", 1), base_row[:, :], start=True, stop=True)\
                .then_inc(range_t, 1)
            turn(0)
            pe.wait_ge(turn_copied[0], NG)
            edges(0)
            pe.wait_ge(sums_done[0], 1)
            for c, (a, w) in enumerate(Z_CHUNKS):
                if c >= 2:
                    pe.wait_ge(z_copied, c - 1)
                pe.matmul(ps_node[c % 2][0:D, 0:w], prm("w1", D), agg[:, a:a + w], start=True, stop=True)\
                    .then_inc(z_done, 1)
            pe.wait_ge(z_copied, len(Z_CHUNKS))
            pe.wait_ge(ones_set, 1)
            for g, (j, m) in enumerate(GROUPS):
                pe.wait_ge(bn_h, g + 1)
                if g >= 2:
                    pe.wait_ge(x1_done, g - 1)
                for i in range(m):
                    last = pe.matmul(ps_node[g % 2][0:NODE_P, i * D:(i + 1) * D], hT[:, j + i, :],
                                     prm("w2", D + 1), start=True, stop=True)
                last.then_inc(w2_done, 1)
            turn(1)
            pe.wait_ge(x1_done, NG)
            for g, (j, m) in enumerate(GROUPS):
                pe.wait_ge(turn_copied[1], g + 1)
                if g >= 2:
                    pe.wait_ge(rows_ready[1], g - 1)
                for i in range(m):
                    last = pe.matmul(ps_node[g % 2][0:NODE_P, i * D:(i + 1) * D], hT[:, j + i, :],
                                     prm("m_node", D + 1), start=True, stop=True)
                last.then_inc(table_mm, 1)
            edges(1)
            pe.wait_ge(sums_done[1], 1)
            pe.wait_ge(rows_ready[1], NG)
            for g, (j, m) in enumerate(GROUPS):
                if g >= 2:
                    pe.wait_ge(result_ready, g - 1)
                for i in range(m):
                    pe.matmul(ps_node[g % 2][0:NODE_P, i * D:(i + 1) * D], hT[:, j + i, :],
                              prm("u_node", D + 1), start=True, stop=False)
                    last = pe.matmul(ps_node[g % 2][0:NODE_P, i * D:(i + 1) * D], agg_nodes[:, j + i, :],
                                     prm("u_sum", D), start=False, stop=True)
                last.then_inc(u_done, 1)

        @block.vector
        def _(dve):
            for e in edge_sems:
                for s in range(2):
                    dve.sem_inc(e.added[s], 1)
                    dve.sem_inc(e.accumulated[s], 1)

            def spread(v, m):
                return v.unsqueeze(2).broadcast_to([NODE_P, m, D])

            def layer_norm(layer):
                for g, (j, m) in enumerate(GROUPS):
                    if layer == 0:
                        dve.wait_ge(x_landed, 16 * NG)
                    else:
                        dve.wait_ge(x1_done, g + 1)
                    dve.tensor_reduce(ln_sum[:, j:j + m], xs[:, j:j + m, :], AX_X, ALU.add)\
                        .then_inc(summed[layer], 1)
                if layer == 1:
                    dve.wait_ge(turned[0], NG)
                for g, (j, m) in enumerate(GROUPS):
                    dve.wait_ge(summed[layer], g + 1)
                    dve.scalar_tensor_tensor(out=xc[:, j:j + m, :], in0=spread(ln_sum[:, j:j + m], m),
                                             scalar=-1.0 / D, in1=xs[:, j:j + m, :], op0=ALU.mult, op1=ALU.add)\
                        .then_inc(centred[layer], 1)
                for g, (j, m) in enumerate(GROUPS):
                    dve.wait_ge(squared[layer], g + 1)
                    dve.tensor_reduce(ln_var[:, j:j + m], sq[:, j:j + m, :], AX_X, ALU.add)\
                        .then_inc(var_done[layer], 1)
                for g, (j, m) in enumerate(GROUPS):
                    dve.wait_ge(std_done[layer], g + 1)
                    dve.reciprocal(ln_inv[:, j:j + m], ln_std[:, j:j + m]).then_inc(inv_done[layer], 1)
                for g, (j, m) in enumerate(GROUPS):
                    dve.wait_ge(inv_done[layer], g + 1)
                    dve.scalar_tensor_tensor(out=xc[:, j:j + m, :], in0=xc[:, j:j + m, :], scalar=0.0,
                                             in1=spread(ln_inv[:, j:j + m], m), op0=ALU.max, op1=ALU.mult)\
                        .then_inc(normed[layer], 1)

            def window_starts():
                dve.wait_ge(dst_landed, 16)
                dve.tensor_copy(rel[:, :], dst_int[:, :]).then_inc(range_v, 1)
                for i, op in enumerate((ALU.min, ALU.max)):
                    dve.wait_ge(range_v, 1)
                    dve.tensor_reduce(ext[:, i, :], rel[:, :].rearrange("p (b t) -> p b t", t=BATCH), AX_X, op)\
                        .then_inc(range_v, 1)
                dve.wait_ge(range_t, 1)
                for i, op in enumerate((ALU.min, ALU.max)):
                    dve.tensor_reduce(lohi[0:BATCHES, i:i + 1], ps_node[0][0:BATCHES, P * i:P * i + P], AX_X, op)\
                        .then_inc(range_v, 1)
                dve.wait_ge(range_v, 5)
                dve.tensor_tensor(lohi[0:BATCHES, 2:3], lohi[0:BATCHES, 1:2], lohi[0:BATCHES, 0:1], ALU.subtract)\
                    .then_inc(range_v, 1)
                dve.wait_ge(range_t, 2)
                dve.tensor_reduce(flags[:, 0:1], ps_node[1][0:1, P:P + BATCHES], AX_X, ALU.max).then_inc(range_v, 1)
                dve.wait_ge(range_v, 7)
                dve.tensor_scalar(flags[:, 1:2], flags[:, 0:1], float(WINDOW), None, ALU.is_lt).then_inc(range_v, 1)
                dve.tensor_scalar(flags[:, 2:3], flags[:, 0:1], float(WINDOW), None, ALU.is_ge).then_inc(range_v, 1)
                dve.wait_ge(range_v, 8)
                dve.tensor_scalar(base_row[:, :], ps_node[1][0:1, 0:BATCHES], flags[:, 1:2], None, ALU.mult)\
                    .then_inc(range_v, 1)
                dve.wait_ge(range_v, 10)
                dve.tensor_copy(flag_int[:, :], flags[:, 2:3]).then_inc(windows_set, 1)
                dve.tensor_copy(base_int[:, :], base_row[:, :]).then_inc(windows_set, 1)
                dve.wait_ge(range_t, 3)
                dve.tensor_tensor(rel[:, :].rearrange("p (b t) -> p b t", t=BATCH),
                                  rel[:, :].rearrange("p (b t) -> p b t", t=BATCH),
                                  ps_node[0][:, 0:BATCHES].unsqueeze(2).broadcast_to([P, BATCHES, BATCH]),
                                  ALU.subtract).then_inc(windows_set, 1)
                dve.wait_ge(windows_set, 3)
                dve.sem_inc(windows_ready, 1)

            def copy_idx(layer, s, batch):
                dve.tensor_copy(idx_slot[:, s, :], idx_all[:, bass.ds(batch * BATCH, BATCH)])\
                    .then_inc(edge_sems[layer].idx_ready[s], 1)

            def edges(layer):
                e = edge_sems[layer]

                def one_pair(k, n):
                    for s in range(2):
                        batch = k * 2 + s
                        dve.wait_ge(e.scattered[s], freed(n))
                        dve.tensor_tensor(onehot[:, s, :, :],
                                          prm("iota").unsqueeze(1).broadcast_to([P, BATCH, WINDOW]),
                                          rel[:, bass.ds(batch * BATCH, BATCH)].unsqueeze(2)
                                          .broadcast_to([P, BATCH, WINDOW]),
                                          ALU.is_equal).then_inc(e.onehot_done[s], 1)
                        dve.wait_ge(e.rows_landed[s], (n + 1) * 16 * BATCH)
                        dve.wait_ge(e.projected[s], done(n))
                        dve.wait_ge(e.relu_done[s], freed(n))
                        dve.tensor_tensor(pre[:, s, :], ps_edge[s][:, 0:BATCH * D], rows[:, s, :], ALU.add)\
                            .then_inc(e.added[s], 1)
                        copy_idx(layer, s, batch + 2)
                        start = dve.value_load(base_int[0:1, bass.ds(batch, 1)], min_val=0, max_val=N)
                        dve.wait_ge(e.scattered[s], done(n))
                        dve.wait_ge(e.accumulated[1 - s], done(n) if s else freed(n))
                        dve.tensor_tensor(agg[:, bass.ds(start, WINDOW)], agg[:, bass.ds(start, WINDOW)],
                                          ps_win[s][0:D, 0:WINDOW], ALU.add).then_inc(e.accumulated[s], 1)

                def move_windows(by, at):
                    dve.tensor_scalar(rel[:, :], rel[:, :], -float(by), None, ALU.add).then_inc(pass_set[layer], 1)
                    dve.tensor_scalar(base_row[:, :], base_row[:, :], float(by), None, ALU.add)\
                        .then_inc(pass_set[layer], 1)
                    dve.wait_ge(pass_set[layer], at + 2)
                    dve.tensor_copy(base_int[:, :], base_row[:, :]).then_inc(pass_set[layer], 1)
                    dve.wait_ge(pass_set[layer], at + 3)
                    dve.sem_inc(e.pass_begun, 1)

                def next_pass(q):
                    dve.wait_ge(e.accumulated[1], q * PAIRS + 1)
                    move_windows(WINDOW, (q - 1) * 3)

                def first_pass_again():
                    dve.wait_ge(e.accumulated[1], PASSES * PAIRS + 1)
                    move_windows(-WINDOW * (PASSES - 1), (PASSES - 1) * 3)

                edge_passes(dve, one_pair, next_pass, first_pass_again)

            dve.wait_ge(idx_landed, 16)
            for s in range(2):
                copy_idx(0, s, s)
            layer_norm(0)
            window_starts()
            dve.wait_ge(turn_copied[0], NG)
            dve.wait_ge(sums_ready[0], 1)
            edges(0)
            dve.drain().then_inc(sums_done[0], 1)
            dve.wait_ge(sums_done[0], 1)
            for s in range(2):
                copy_idx(1, s, s)
            for c in range(N // STAT_CHUNK):
                a = c * STAT_CHUNK
                dve.wait_ge(z_copied, (a + STAT_CHUNK - 1) // Z_CHUNK + 1)
                dve.bn_stats(bn[:, c, :], zT[:, a:a + STAT_CHUNK]).then_inc(bn_stat, 1)
            dve.wait_ge(bn_stat, N // STAT_CHUNK)
            dve.bn_aggr(bn_mv[:, :], bn[:, :, :]).then_inc(bn_v, 1)
            dve.wait_ge(bn_std, 1)
            dve.reciprocal(bn_t[:, 1:2], bn_t[:, 0:1]).then_inc(bn_v, 1)
            dve.wait_ge(bn_v, 2)
            dve.tensor_tensor(bn_t[:, 2:3], bn_t[:, 1:2], prm("gamma", D), ALU.mult).then_inc(bn_v, 1)
            dve.wait_ge(bn_v, 3)
            dve.tensor_tensor(bn_t[:, 3:4], bn_t[:, 2:3], bn_mv[:, 0:1], ALU.mult).then_inc(bn_v, 1)
            dve.wait_ge(bn_v, 4)
            dve.tensor_tensor(bn_t[:, 4:5], prm("beta", D), bn_t[:, 3:4], ALU.subtract).then_inc(bn_v, 1)
            for g, (j, m) in enumerate(GROUPS):
                dve.wait_ge(w2_done, g + 1)
                dve.tensor_tensor(xs[:, j:j + m, :], xs[:, j:j + m, :],
                                  ps_node[g % 2][0:NODE_P, 0:m * D].rearrange("p (j d) -> p j d", d=D), ALU.add)\
                    .then_inc(x1_done, 1)
            layer_norm(1)
            for g, (j, m) in enumerate(GROUPS):
                dve.wait_ge(table_mm, g + 1)
                dve.tensor_copy(sq[:, j:j + m, :],
                                ps_node[g % 2][0:NODE_P, 0:m * D].rearrange("p (j d) -> p j d", d=D))\
                    .then_inc(rows_ready[1], 1)
            dve.wait_ge(sums_ready[1], 1)
            edges(1)
            dve.drain().then_inc(sums_done[1], 1)
            for g, (j, m) in enumerate(GROUPS):
                dve.wait_ge(u_done, g + 1)
                dve.scalar_tensor_tensor(out=xc[:, j:j + m, :],
                                         in0=ps_node[g % 2][0:NODE_P, 0:m * D].rearrange("p (j d) -> p j d", d=D),
                                         scalar=0.0, in1=xs[:, j:j + m, :], op0=ALU.max, op1=ALU.add)\
                    .then_inc(result_ready, 1)


def laid_out(x, src, dst, edge_attr_16, edge_attr_64, L0_gnn_W_edge, L0_gnn_b_edge, L0_gnn_W1, L0_gnn_b1,
             L0_gnn_gamma, L0_gnn_beta, L0_gnn_W2, L0_gnn_b2, L1_gnn_M_W, L1_gnn_M_b, L1_gnn_U_W, L1_gnn_U_b):
    def tiles(a, fill):
        padded = np.full(TILES * P, fill, np.int32)
        padded[:EDGES] = a
        return padded.reshape(TILES, P).T

    def features(a):
        padded = np.zeros((TILES * P, a.shape[1]), np.float32)
        padded[:EDGES] = a
        return np.ascontiguousarray(padded.reshape(BATCHES, BATCH * P, -1).transpose(0, 2, 1))

    params = np.zeros((P, PARAM_COLS), np.float32)

    def put(name, block):
        params[:block.shape[0], PARAMS[name]] = block

    put("identity", np.eye(P, dtype=np.float32))
    put("iota", np.tile(np.arange(WINDOW, dtype=np.float32), (P, 1)))
    put("ones", np.ones((1, P), np.float32))
    put("eps", np.full((P, 1), LN_EPS, np.float32))
    put("w_edge", L0_gnn_W_edge.T)
    put("b_edge", np.tile(L0_gnn_b_edge, (P, 1)))
    put("w1", L0_gnn_W1.T)
    put("w2", np.concatenate([L0_gnn_W2.T, L0_gnn_b2[None]]))
    put("m_node", np.concatenate([L1_gnn_M_W[:, :D].T, L1_gnn_M_b[None]]))
    put("m_edge", L1_gnn_M_W[:, D:].T)
    put("u_node", np.concatenate([L1_gnn_U_W[:, :D].T, L1_gnn_U_b[None]]))
    put("u_sum", L1_gnn_U_W[:, D:].T)
    put("b1", L0_gnn_b1[:, None])
    put("gamma", L0_gnn_gamma[:, None])
    put("beta", L0_gnn_beta[:, None])
    idx = tiles(src, 0)
    return {
        "x": np.ascontiguousarray(x).reshape(NODE_P, NODE_COLS, D),
        "idx": np.ascontiguousarray(np.concatenate([idx, idx[:, :2 * BATCH]], axis=1)),
        "dst": np.ascontiguousarray(tiles(dst, N)),
        "attr0": features(edge_attr_16),
        "attr1": features(edge_attr_64),
        "params": params,
    }


def kernel(**inputs):
    import concourse.bacc as bacc
    from concourse.bass_utils import run_bass_kernel_spmd

    arrays = laid_out(**{name: np.asarray(a) for name, a in inputs.items()})
    nc = bacc.Bacc("TRN2", target_bir_lowering=False, num_devices=1)
    ins = [nc.dram_tensor(name, a.shape, mybir.dt.from_np(a.dtype), kind="ExternalInput").ap()
           for name, a in arrays.items()]
    out = nc.dram_tensor("out", (NODE_P, NODE_COLS, D), F32, kind="ExternalOutput").ap()
    build(nc, *ins, out)
    result = run_bass_kernel_spmd(nc, [arrays], core_ids=[0])
    return result.results[0]["out"].reshape(N, D)
```

```python
from contextlib import ExitStack

import numpy as np

import concourse.bass as bass
from concourse import mybir

F32 = mybir.dt.float32
I32 = mybir.dt.int32
ALU = mybir.AluOpType
ACT = mybir.ActivationFunctionType
AX_X = mybir.AxisListType.X

N = 6250
D = 64
EDGES = 206250
EDGE_DIM = (16, 64)
NODE_P = 125
NODE_COLS = N // NODE_P
P = 128
BATCH = 13
TILES = 1612
BATCHES = TILES // BATCH
PAIRS = BATCHES // 2
WINDOW = 64
PASSES = -(-N // WINDOW)
ACC_COLS = N + WINDOW + 6
GROUP = 8
GROUPS = [(j, min(GROUP, NODE_COLS - j)) for j in range(0, NODE_COLS, GROUP)]
NG = len(GROUPS)
COL_PAIRS = NODE_COLS // 2
START_GROUP = 4
START_GROUPS = [(q, min(START_GROUP, COL_PAIRS - q)) for q in range(0, COL_PAIRS, START_GROUP)]
STAT_CHUNK = 500
STAT_CHUNKS = [(c, min(STAT_CHUNK, N - c)) for c in range(0, N, STAT_CHUNK)]
LN_EPS = 1e-5
BN_EPS = 1e-5

assert NODE_P * NODE_COLS == N and TILES * P >= EDGES and BATCHES * BATCH == TILES and BATCHES % 2 == 0
assert BATCHES <= P

PARAMS = {}
PARAM_COLS = 0
for _name, _width in (("identity", P), ("iota", WINDOW), ("ones", P), ("w_edge", D), ("b_edge", D), ("b2", D), ("m_b", D), ("w1_twice", 2 * D),
                      ("w2_twice", 2 * D), ("m_node_twice", 2 * D), ("m_edge", D), ("u_node_twice", 2 * D), ("u_sum", D),
                      ("b1", 1), ("u_b", 1), ("gamma", 1), ("beta", 1), ("eps", 1)):
    PARAMS[_name] = slice(PARAM_COLS, PARAM_COLS + _width)
    PARAM_COLS += _width


class EdgeSems:

    def __init__(self, sem, layer):
        def pair(what):
            return [sem(f"{what}_l{layer}_s{s}") for s in range(2)]

        self.idx_ready = pair("idx_ready")
        self.gathers_begun = sem(f"gathers_begun_l{layer}")
        self.weighting_begun = sem(f"weighting_begun_l{layer}")
        self.pass_begun = sem(f"pass_begun_l{layer}")
        self.rows_landed = pair("rows_landed")
        self.attr_landed = pair("attr_landed")
        self.projected = pair("projected")
        self.added = pair("added")
        self.relu_done = pair("relu_done")
        self.onehot_done = pair("onehot_done")
        self.scattered = pair("scattered")
        self.window_copied = pair("window_copied")
        self.weighted = pair("weighted")
        self.accumulated = pair("accumulated")


def done(k):
    return k + 2


def freed(k):
    return k + 1


def build(nc, x, idx, dst, attr0, attr1, params, out):
    attrs = (attr0, attr1)
    table = [nc.dram_tensor(f"node_table_l{layer}", (N, D), F32, kind="Internal").ap() for layer in range(2)]
    with ExitStack() as ctx:
        def sb(name, shape, dt=F32):
            return ctx.enter_context(nc.sbuf_tensor(name, shape, dt))

        def ps(name, shape):
            return ctx.enter_context(nc.psum_tensor(name, shape, F32))

        def sem(name):
            return ctx.enter_context(nc.semaphore(name))

        par = sb("par", [P, PARAM_COLS])
        idx_all = sb("idx_all", [P, TILES + 2 * BATCH], I32)
        dst_int = sb("dst_int", [P, TILES], I32)
        rel = sb("rel", [P, TILES])
        idx_slot = sb("idx_slot", [P, 2, BATCH], I32)
        rows = sb("rows", [P, 2, BATCH * D])
        attr_buf = sb("attr_buf", [D, 2, BATCH * P])
        pre = sb("pre", [P, 2, BATCH * D])
        msg = sb("msg", [P, 2, BATCH * D])
        onehot = sb("onehot", [P, 2, BATCH, WINDOW])
        window = sb("window", [D, 2, WINDOW])
        acc = sb("acc", [D, ACC_COLS])
        zh = sb("zh", [2 * D, COL_PAIRS, NODE_P])
        hT = sb("hT", [2 * D, COL_PAIRS, NODE_P])
        xs = sb("xs", [NODE_P, NODE_COLS, D])
        xc = sb("xc", [NODE_P, NODE_COLS, D])
        sq = sb("sq", [NODE_P, NODE_COLS, D])
        ln_sum = sb("ln_sum", [NODE_P, NODE_COLS])
        ln_mean = sb("ln_mean", [NODE_P, NODE_COLS])
        ln_var = sb("ln_var", [NODE_P, NODE_COLS])
        ln_std = sb("ln_std", [NODE_P, NODE_COLS])
        ln_inv = sb("ln_inv", [NODE_P, NODE_COLS])
        ext = sb("ext", [P, 2, BATCHES])
        lohi = sb("lohi", [P, 4])
        base_row = sb("base_row", [1, BATCHES])
        base_int = sb("base_int", [1, BATCHES], I32)
        spare = sb("spare", [1, 2])
        flags = sb("flags", [1, 4])
        flag_int = sb("flag_int", [1, 1], I32)
        bn = sb("bn", [D, len(STAT_CHUNKS), nc.vector.BN_STATS_DIM])
        bn_mv = sb("bn_mv", [D, nc.vector.BN_AGGR_DIM])
        bn_t = sb("bn_t", [D, 6])

        ps_edge = [ps(f"ps_edge{s}", [P, 1024]) for s in range(2)]
        ps_win = [ps(f"ps_win{s}", [P, 512]) for s in range(2)]
        ps_node = [ps(f"ps_node{s}", [P, 512]) for s in range(2)]

        acc_pairs = acc[:, 0:N].rearrange("f (p q h) -> f h q p", h=2, q=COL_PAIRS)
        acc_nodes = acc[:, 0:N].rearrange("f (p j) -> f j p", j=NODE_COLS)

        ps_post = ps_node[0][0:D, 0:WINDOW]
        iota = ps_node[1][:, 0:WINDOW]

        def prm(name, rows_n=P):
            return par[0:rows_n, PARAMS[name]]

        par_landed = sem("par_landed")
        x_landed = [sem(f"x_landed{g}") for g in range(NG)]
        dst_landed = sem("dst_landed")
        idx_landed = sem("idx_landed")
        range_v = sem("range_v")
        range_t = sem("range_t")
        windows_set = sem("windows_set")
        windows_ready = sem("windows_ready")

        def per_layer(what):
            return [sem(f"{what}_l{layer}") for layer in range(2)]

        summed = per_layer("summed")
        mean_done = per_layer("mean_done")
        centred = per_layer("centred")
        squared = per_layer("squared")
        var_done = per_layer("var_done")
        std_done = per_layer("std_done")
        inv_done = per_layer("inv_done")
        normed = per_layer("normed")
        turned = per_layer("turned")
        turn_copied = per_layer("turn_copied")
        rows_ready = per_layer("rows_ready")
        table_stored = per_layer("table_stored")
        start_mm = per_layer("start_mm")
        started = per_layer("started")
        sums_done = per_layer("sums_done")
        margin_set = sem("margin_set")
        pass_set = per_layer("pass_set")
        bn_stat = sem("bn_stat")
        bn_v = sem("bn_v")
        bn_std = sem("bn_std")
        bn_h = sem("bn_h")
        spare_set = sem("spare_set")
        iota_set = sem("iota_set")
        b2_added = sem("b2_added")
        w2_done = sem("w2_done")
        x1_done = sem("x1_done")
        table_mm = sem("table_mm")
        u_turned = sem("u_turned")
        result_ready = sem("result_ready")
        out_stored = sem("out_stored")
        edge_sems = [EdgeSems(sem, layer) for layer in range(2)]

        block = ctx.enter_context(nc.Block())

        def spread(v, m):
            return v.unsqueeze(2).broadcast_to([NODE_P, m, D])

        def edge_passes(eng, one_pair, first_step=None, last_step=None):
            with eng.Fori(0, PAIRS) as k:
                one_pair(k, k)
            eng.wait_ge(windows_ready, 1)
            more = eng.value_load(flag_int[0:1, 0:1], min_val=0, max_val=1)
            with eng.If(more > 0):
                with eng.Fori(1, PASSES) as q:
                    if first_step is not None:
                        first_step(q)
                    with eng.Fori(0, PAIRS) as k:
                        one_pair(k, q * PAIRS + k)
                if last_step is not None:
                    last_step()
                eng.nop()
            with eng.Else():
                eng.nop()
            eng.nop()

        @block.sync
        def _(sp):
            for g, (j, m) in enumerate(GROUPS):
                sp.dma_start(xs[:, j:j + m, :], x[:, j:j + m, :]).then_inc(x_landed[g], 16)
            for layer in range(2):
                e, kd = edge_sems[layer], EDGE_DIM[layer]
                rows_of = table[layer].rearrange("(p j) d -> p j d", j=NODE_COLS)
                for g, (j, m) in enumerate(GROUPS):
                    sp.wait_ge(rows_ready[layer], g + 1)
                    sp.dma_start(rows_of[:, j:j + m, :], sq[:, j:j + m, :]).then_inc(table_stored[layer], 16)

                def one_pair(k, n):
                    for s in range(2):
                        sp.wait_ge(e.projected[s], freed(n))
                        sp.dma_start(attr_buf[0:kd, s, :],
                                     attrs[layer][bass.ds(k * 2 + s, 1)].rearrange("a d e -> (a d) e"))\
                            .then_inc(e.attr_landed[s], 16)

                edge_passes(sp, one_pair)
            for g, (j, m) in enumerate(GROUPS):
                sp.wait_ge(result_ready, g + 1)
                sp.dma_start(out[:, j:j + m, :], xc[:, j:j + m, :]).then_inc(out_stored, 16)
            sp.wait_ge(out_stored, 16 * NG)

        @block.gpsimd
        def _(pool):
            pool.memset(acc[:, N:ACC_COLS], 0.0).then_inc(margin_set, 1)
            pool.wait_ge(margin_set, 1)

            def centre(layer, g):
                j, m = GROUPS[g]
                pool.wait_ge(mean_done[layer], g + 1)
                pool.tensor_tensor(xc[:, j:j + m, :], xs[:, j:j + m, :], spread(ln_mean[:, j:j + m], m),
                                   ALU.subtract).then_inc(centred[layer], 1)

            for step in range(NG + 1):
                if step < NG:
                    centre(0, step)
                if step >= 1:
                    j, m = GROUPS[step - 1]
                    pool.wait_ge(par_landed, 16)
                    pool.wait_ge(normed[0], step)
                    pool.tensor_tensor(sq[:, j:j + m, :], xc[:, j:j + m, :],
                                       prm("b_edge", NODE_P).unsqueeze(1).broadcast_to([NODE_P, m, D]), ALU.add)\
                        .then_inc(rows_ready[0], 1)
            for layer in range(2):
                e = edge_sems[layer]
                if layer == 1:
                    pool.wait_ge(turned[0], NG)
                    for g in range(NG):
                        centre(1, g)

                def one_pair(k, n):
                    for s in range(2):
                        pool.wait_ge(e.idx_ready[s], n + 1)
                        pool.wait_ge(e.added[s], freed(n))
                        pool.sem_inc(e.gathers_begun, 1)
                        for t in range(BATCH):
                            pool.indirect_dma_start(
                                out=rows[:, s, t * D:(t + 1) * D], out_offset=None, in_=table[layer],
                                in_offset=bass.IndirectOffsetOnAxis(ap=idx_slot[:, s, t:t + 1], axis=0),
                            ).then_inc(e.rows_landed[s], 16)

                pool.wait_ge(table_stored[layer], 16 * NG)
                edge_passes(pool, one_pair)

        @block.scalar
        def _(act):
            for e in edge_sems:
                for s in range(2):
                    act.sem_inc(e.relu_done[s], 1)
                    act.sem_inc(e.window_copied[s], 1)
            act.dma_start(par[:, :], params).then_inc(par_landed, 16)
            act.dma_start(dst_int[:, :], dst).then_inc(dst_landed, 16)
            act.dma_start(idx_all[:, :], idx).then_inc(idx_landed, 16)
            act.wait_ge(spare_set, 1)
            act.activation(spare[:, 1:2], spare[:, 0:1], ACT.Sqrt)
            act.wait_ge(par_landed, 16)

            def square(layer, g):
                j, m = GROUPS[g]
                act.wait_ge(centred[layer], g + 1)
                act.activation(sq[:, j:j + m, :], xc[:, j:j + m, :], ACT.Square).then_inc(squared[layer], 1)

            def root(layer, g):
                j, m = GROUPS[g]
                act.wait_ge(var_done[layer], g + 1)
                act.activation(ln_std[:, j:j + m], ln_var[:, j:j + m], ACT.Sqrt,
                               bias=prm("eps", NODE_P), scale=1.0 / D).then_inc(std_done[layer], 1)

            def copy_turned(layer, g):
                j, m = GROUPS[g]
                act.wait_ge(turned[layer], g + 1)
                act.activation(hT[:, j // 2:(j + m) // 2, :],
                               ps_edge[g % 2][:, 0:512].rearrange("f (q p) -> f q p", p=P)[:, 0:m // 2, 0:NODE_P],
                               ACT.Copy).then_inc(turn_copied[layer], 1)

            def start_acc(layer):
                for c, (q, m) in enumerate(START_GROUPS):
                    act.wait_ge(start_mm[layer], c + 1)
                    for h in range(2):
                        half = slice(h * D, (h + 1) * D)
                        act.activation(acc_pairs[:, h, q:q + m, :],
                                       ps_node[c % 2][half, 0:m * NODE_P].rearrange("f (q p) -> f q p", p=NODE_P),
                                       ACT.Identity, bias=par[half, PARAMS[("b1", "u_b")[layer]]])\
                            .then_inc(started[layer], 1)

            def edges(layer):
                e = edge_sems[layer]

                def one_pair(k, n):
                    for s in range(2):
                        act.wait_ge(e.added[s], done(n))
                        act.wait_ge(e.scattered[s], freed(n))
                        act.activation(msg[:, s, :], pre[:, s, :], ACT.Relu).then_inc(e.relu_done[s], 1)
                        act.wait_ge(e.scattered[s], done(n))
                        act.wait_ge(e.weighted[s], freed(n))
                        act.activation(window[:, s, :], ps_win[s][0:D, 0:WINDOW], ACT.Copy)\
                            .then_inc(e.window_copied[s], 1)

                edge_passes(act, one_pair)

            for step in range(NG + 1):
                if step >= 1:
                    root(0, step - 1)
                if step < NG:
                    square(0, step)
            for g in range(NG):
                copy_turned(0, g)
            start_acc(0)
            edges(0)
            act.wait_ge(bn_v, 1)
            act.activation(bn_t[:, 0:1], bn_mv[:, 1:2], ACT.Sqrt, bias=prm("eps", D)).then_inc(bn_std, 1)
            act.wait_ge(bn_v, 5)
            act.wait_ge(table_stored[0], 16 * NG)
            for step in range(-1, NG + 2):
                if step + 1 < NG:
                    j, m = GROUPS[step + 1]
                    for h in range(2):
                        act.activation(zh[h * D:(h + 1) * D, j // 2:(j + m) // 2, :],
                                       acc_pairs[:, h, j // 2:(j + m) // 2, :], ACT.Relu,
                                       scale=bn_t[:, 2:3], bias=bn_t[:, 4:5]).then_inc(bn_h, 1)
                if step >= 2:
                    copy_turned(1, step - 2)
                if 1 <= step <= NG:
                    root(1, step - 1)
                if 0 <= step < NG:
                    square(1, step)
            act.wait_ge(bn_h, 2 * NG)
            start_acc(1)
            edges(1)

        @block.tensor
        def _(pe):
            for e in edge_sems:
                for s in range(2):
                    pe.sem_inc(e.projected[s], 1)
                    pe.sem_inc(e.scattered[s], 1)
                    pe.sem_inc(e.weighted[s], 1)
            pe.wait_ge(par_landed, 16)

            def turn(layer, g):
                j, m = GROUPS[g]
                pe.wait_ge(normed[layer], g + 1)
                if g >= 2:
                    pe.wait_ge(turn_copied[layer], g - 1)
                for i in range(m // 2):
                    last = pe.transpose(ps_edge[g % 2][:, i * P:i * P + NODE_P],
                                        xc[:, j + 2 * i:j + 2 * i + 2, :].rearrange("p h d -> p (h d)"),
                                        prm("identity", NODE_P)[:, 0:NODE_P])
                last.then_inc(turned[layer], 1)

            def node_rows(to, features, weights, g):
                j, m = GROUPS[g]
                for i in range(m // 2):
                    last = pe.matmul(to[0:NODE_P, 2 * i * D:2 * (i + 1) * D], features[:, j // 2 + i, :],
                                     prm(weights), start=True, stop=True)
                return last

            def start_acc(layer):
                for c, (q, m) in enumerate(START_GROUPS):
                    if c >= 2:
                        pe.wait_ge(started[layer], 2 * (c - 1))
                    pe.matmul(ps_node[c % 2][:, 0:m * NODE_P], prm(("w1_twice", "u_node_twice")[layer]),
                              hT[:, q:q + m, :], start=True, stop=True).then_inc(start_mm[layer], 1)
                pe.wait_ge(started[layer], 2 * len(START_GROUPS))

            def edges(layer):
                e, kd = edge_sems[layer], EDGE_DIM[layer]
                weights = prm(("w_edge", "m_edge")[layer], kd)

                def one_pair(k, n):
                    for s in range(2):
                        pe.wait_ge(e.attr_landed[s], (n + 1) * 16)
                        pe.wait_ge(e.added[s], freed(n))
                        for t in range(BATCH):
                            last = pe.matmul(ps_edge[s][:, t * D:(t + 1) * D],
                                             attr_buf[0:kd, s, t * P:(t + 1) * P], weights,
                                             start=True, stop=True)
                        last.then_inc(e.projected[s], 1)
                        pe.wait_ge(e.relu_done[s], done(n))
                        pe.wait_ge(e.onehot_done[s], n + 1)
                        pe.wait_ge(e.window_copied[s], freed(n))
                        for t in range(BATCH):
                            last = pe.matmul(ps_win[s][0:D, 0:WINDOW], msg[:, s, t * D:(t + 1) * D],
                                             onehot[:, s, t, :], start=(t == 0), stop=(t == BATCH - 1))
                        last.then_inc(e.scattered[s], 1)
                        pe.wait_ge(e.window_copied[s], done(n))
                        pe.wait_ge(e.accumulated[1 - s], done(n) if s else freed(n))
                        pe.sem_inc(e.weighting_begun, 1)
                        pe.matmul(ps_post, prm(("w1_twice", "u_sum")[layer], D)[:, 0:D], window[:, s, :],
                                  start=True, stop=True).then_inc(e.weighted[s], 1)

                edge_passes(pe, one_pair)

            for g in range(NG):
                turn(0, g)
            pe.wait_ge(range_v, 3)
            for i in range(2):
                last = pe.transpose(ps_win[0][0:BATCHES, P * i:P * i + P], ext[:, i, :], prm("identity"))
            last.then_inc(range_t, 1)
            pe.wait_ge(range_v, 6)
            for i in range(2):
                last = pe.transpose(ps_win[1][0:1, P * i:P * i + BATCHES], lohi[0:BATCHES, 2 * i:2 * i + 1],
                                    prm("identity", BATCHES)[:, 0:BATCHES])
            last.then_inc(range_t, 1)
            pe.wait_ge(range_v, 10)
            pe.matmul(ps_win[0][:, 0:BATCHES], prm("ones", 1), base_row[:, :], start=True, stop=True)\
                .then_inc(range_t, 1)
            pe.wait_ge(turn_copied[0], NG)
            start_acc(0)
            pe.wait_ge(windows_ready, 1)
            edges(0)
            pe.wait_ge(sums_done[0], 1)
            for step in range(-1, NG + 2):
                if step >= 2:
                    turn(1, step - 2)
                if step + 1 < NG:
                    g = step + 1
                    pe.wait_ge(bn_h, 2 * (g + 1))
                    if g >= 2:
                        pe.wait_ge(x1_done, g - 1)
                    node_rows(ps_node[g % 2], zh, "w2_twice", g).then_inc(w2_done, 1)
                if step >= 2:
                    g = step - 2
                    pe.wait_ge(turn_copied[1], g + 1)
                    if g >= 2:
                        pe.wait_ge(rows_ready[1], g - 1)
                    node_rows(ps_win[g % 2], hT, "m_node_twice", g).then_inc(table_mm, 1)
            pe.wait_ge(x1_done, NG)
            start_acc(1)
            pe.wait_ge(rows_ready[1], NG)
            edges(1)
            pe.wait_ge(sums_done[1], 1)
            for g, (j, m) in enumerate(GROUPS):
                if g >= 2:
                    pe.wait_ge(result_ready, g - 1)
                for i in range(m):
                    last = pe.transpose(ps_node[g % 2][0:NODE_P, i * D:(i + 1) * D], acc_nodes[:, j + i, :],
                                        prm("identity", D)[:, 0:D])
                last.then_inc(u_turned, 1)

        @block.vector
        def _(dve):
            for e in edge_sems:
                for s in range(2):
                    dve.sem_inc(e.added[s], 1)
                    dve.sem_inc(e.accumulated[s], 1)

            def mean(layer, g):
                j, m = GROUPS[g]
                dve.tensor_reduce(ln_sum[:, j:j + m], xs[:, j:j + m, :], AX_X, ALU.add).then_inc(summed[layer], 1)
                dve.wait_ge(summed[layer], g + 1)
                dve.tensor_scalar(ln_mean[:, j:j + m], ln_sum[:, j:j + m], 1.0 / D, None, ALU.mult)\
                    .then_inc(mean_done[layer], 1)

            def variance(layer, g):
                j, m = GROUPS[g]
                dve.wait_ge(squared[layer], g + 1)
                dve.tensor_reduce(ln_var[:, j:j + m], sq[:, j:j + m, :], AX_X, ALU.add).then_inc(var_done[layer], 1)

            def norm(layer, g):
                j, m = GROUPS[g]
                dve.wait_ge(std_done[layer], g + 1)
                dve.reciprocal(ln_inv[:, j:j + m], ln_std[:, j:j + m]).then_inc(inv_done[layer], 1)
                dve.wait_ge(inv_done[layer], g + 1)
                dve.scalar_tensor_tensor(out=xc[:, j:j + m, :], in0=xc[:, j:j + m, :], scalar=0.0,
                                         in1=spread(ln_inv[:, j:j + m], m), op0=ALU.max, op1=ALU.mult)\
                    .then_inc(normed[layer], 1)

            def window_starts():
                dve.wait_ge(dst_landed, 16)
                dve.tensor_copy(rel[:, :], dst_int[:, :]).then_inc(range_v, 1)
                for i, op in enumerate((ALU.min, ALU.max)):
                    dve.wait_ge(range_v, 1)
                    dve.tensor_reduce(ext[:, i, :], rel[:, :].rearrange("p (b t) -> p b t", t=BATCH), AX_X, op)\
                        .then_inc(range_v, 1)
                dve.wait_ge(range_t, 1)
                for i, op in enumerate((ALU.min, ALU.max)):
                    dve.tensor_reduce(lohi[0:BATCHES, i:i + 1], ps_win[0][0:BATCHES, P * i:P * i + P], AX_X, op)\
                        .then_inc(range_v, 1)
                dve.wait_ge(range_v, 5)
                dve.tensor_tensor(lohi[0:BATCHES, 2:3], lohi[0:BATCHES, 1:2], lohi[0:BATCHES, 0:1], ALU.subtract)\
                    .then_inc(range_v, 1)
                dve.wait_ge(range_t, 2)
                dve.tensor_reduce(flags[:, 0:1], ps_win[1][0:1, P:P + BATCHES], AX_X, ALU.max).then_inc(range_v, 1)
                dve.wait_ge(range_v, 7)
                dve.tensor_scalar(flags[:, 1:2], flags[:, 0:1], float(WINDOW), None, ALU.is_lt).then_inc(range_v, 1)
                dve.tensor_scalar(flags[:, 2:3], flags[:, 0:1], float(WINDOW), None, ALU.is_ge).then_inc(range_v, 1)
                dve.wait_ge(range_v, 8)
                dve.tensor_scalar(base_row[:, :], ps_win[1][0:1, 0:BATCHES], flags[:, 1:2], None, ALU.mult)\
                    .then_inc(range_v, 1)
                dve.wait_ge(range_v, 10)
                dve.tensor_copy(flag_int[:, :], flags[:, 2:3]).then_inc(windows_set, 1)
                dve.tensor_copy(base_int[:, :], base_row[:, :]).then_inc(windows_set, 1)
                dve.wait_ge(range_t, 3)
                dve.tensor_tensor(rel[:, :].rearrange("p (b t) -> p b t", t=BATCH),
                                  rel[:, :].rearrange("p (b t) -> p b t", t=BATCH),
                                  ps_win[0][:, 0:BATCHES].unsqueeze(2).broadcast_to([P, BATCHES, BATCH]),
                                  ALU.subtract).then_inc(windows_set, 1)
                dve.wait_ge(windows_set, 3)
                dve.sem_inc(windows_ready, 1)

            def set_iota(layer):
                dve.wait_ge(started[layer], 2 * len(START_GROUPS))
                dve.tensor_copy(iota, prm("iota")).then_inc(iota_set, 1)
                dve.wait_ge(iota_set, layer + 1)

            def copy_idx(layer, s, batch):
                dve.tensor_copy(idx_slot[:, s, :], idx_all[:, bass.ds(batch * BATCH, BATCH)])\
                    .then_inc(edge_sems[layer].idx_ready[s], 1)

            def edges(layer):
                e = edge_sems[layer]

                def one_pair(k, n):
                    for s in range(2):
                        batch = k * 2 + s
                        dve.wait_ge(e.scattered[s], freed(n))
                        dve.tensor_tensor(onehot[:, s, :, :],
                                          iota.unsqueeze(1).broadcast_to([P, BATCH, WINDOW]),
                                          rel[:, bass.ds(batch * BATCH, BATCH)].unsqueeze(2)
                                          .broadcast_to([P, BATCH, WINDOW]),
                                          ALU.is_equal).then_inc(e.onehot_done[s], 1)
                        dve.wait_ge(e.rows_landed[s], (n + 1) * 16 * BATCH)
                        dve.wait_ge(e.projected[s], done(n))
                        dve.wait_ge(e.relu_done[s], freed(n))
                        dve.tensor_tensor(pre[:, s, :], ps_edge[s][:, 0:BATCH * D], rows[:, s, :], ALU.add)\
                            .then_inc(e.added[s], 1)
                        copy_idx(layer, s, batch + 2)
                        start = dve.value_load(base_int[0:1, bass.ds(batch, 1)], min_val=0, max_val=N)
                        dve.wait_ge(e.weighted[s], done(n))
                        dve.wait_ge(e.accumulated[1 - s], done(n) if s else freed(n))
                        dve.tensor_tensor(acc[:, bass.ds(start, WINDOW)], acc[:, bass.ds(start, WINDOW)],
                                          ps_post, ALU.add).then_inc(e.accumulated[s], 1)

                def move_windows(by, at):
                    dve.tensor_scalar(rel[:, :], rel[:, :], -float(by), None, ALU.add).then_inc(pass_set[layer], 1)
                    dve.tensor_scalar(base_row[:, :], base_row[:, :], float(by), None, ALU.add)\
                        .then_inc(pass_set[layer], 1)
                    dve.wait_ge(pass_set[layer], at + 2)
                    dve.tensor_copy(base_int[:, :], base_row[:, :]).then_inc(pass_set[layer], 1)
                    dve.wait_ge(pass_set[layer], at + 3)
                    dve.sem_inc(e.pass_begun, 1)

                def next_pass(q):
                    dve.wait_ge(e.accumulated[1], q * PAIRS + 1)
                    move_windows(WINDOW, (q - 1) * 3)

                def first_pass_again():
                    dve.wait_ge(e.accumulated[1], PASSES * PAIRS + 1)
                    move_windows(-WINDOW * (PASSES - 1), (PASSES - 1) * 3)

                edge_passes(dve, one_pair, next_pass, first_pass_again)

            dve.memset(spare[:, 0:1], 0.0).then_inc(spare_set, 1)
            for step in range(NG + 1):
                if step < NG:
                    dve.wait_ge(x_landed[step], 16)
                    mean(0, step)
                if step >= 1:
                    variance(0, step - 1)
                    norm(0, step - 1)
            dve.wait_ge(idx_landed, 16)
            for s in range(2):
                copy_idx(0, s, s)
            window_starts()
            dve.wait_ge(centred[0], NG)
            dve.tensor_tensor(xs[:, :, :], xs[:, :, :],
                              prm("b2", NODE_P).unsqueeze(1).broadcast_to([NODE_P, NODE_COLS, D]), ALU.add)\
                .then_inc(b2_added, 1)
            dve.wait_ge(par_landed, 16)
            set_iota(0)
            dve.wait_ge(margin_set, 1)
            edges(0)
            dve.drain().then_inc(sums_done[0], 1)
            dve.wait_ge(sums_done[0], 1)
            for s in range(2):
                copy_idx(1, s, s)
            for c, (a, w) in enumerate(STAT_CHUNKS):
                dve.bn_stats(bn[:, c, :], acc[:, a:a + w]).then_inc(bn_stat, 1)
            dve.wait_ge(bn_stat, len(STAT_CHUNKS))
            dve.bn_aggr(bn_mv[:, :], bn[:, :, :]).then_inc(bn_v, 1)
            dve.wait_ge(bn_std, 1)
            dve.reciprocal(bn_t[:, 1:2], bn_t[:, 0:1]).then_inc(bn_v, 1)
            dve.wait_ge(bn_v, 2)
            dve.tensor_tensor(bn_t[:, 2:3], bn_t[:, 1:2], prm("gamma", D), ALU.mult).then_inc(bn_v, 1)
            dve.wait_ge(bn_v, 3)
            dve.tensor_tensor(bn_t[:, 3:4], bn_t[:, 2:3], bn_mv[:, 0:1], ALU.mult).then_inc(bn_v, 1)
            dve.wait_ge(bn_v, 4)
            dve.tensor_tensor(bn_t[:, 4:5], prm("beta", D), bn_t[:, 3:4], ALU.subtract).then_inc(bn_v, 1)
            for step in range(NG + 2):
                if step < NG:
                    j, m = GROUPS[step]
                    dve.wait_ge(b2_added, 1)
                    dve.wait_ge(w2_done, step + 1)
                    dve.tensor_tensor(xs[:, j:j + m, :], xs[:, j:j + m, :],
                                      ps_node[step % 2][0:NODE_P, 0:m * D].rearrange("p (j d) -> p j d", d=D),
                                      ALU.add).then_inc(x1_done, 1)
                    dve.wait_ge(x1_done, step + 1)
                    mean(1, step)
                if 1 <= step <= NG:
                    variance(1, step - 1)
                if step == NG:
                    norm(1, step - 1)
                if step >= 2:
                    g = step - 2
                    j, m = GROUPS[g]
                    dve.wait_ge(table_mm, g + 1)
                    dve.tensor_tensor(sq[:, j:j + m, :],
                                      ps_win[g % 2][0:NODE_P, 0:m * D].rearrange("p (j d) -> p j d", d=D),
                                      prm("m_b", NODE_P).unsqueeze(1).broadcast_to([NODE_P, m, D]), ALU.add)\
                        .then_inc(rows_ready[1], 1)
                if 1 <= step < NG:
                    norm(1, step - 1)
            set_iota(1)
            edges(1)
            dve.drain().then_inc(sums_done[1], 1)
            for g, (j, m) in enumerate(GROUPS):
                dve.wait_ge(u_turned, g + 1)
                dve.scalar_tensor_tensor(out=xc[:, j:j + m, :],
                                         in0=ps_node[g % 2][0:NODE_P, 0:m * D].rearrange("p (j d) -> p j d", d=D),
                                         scalar=0.0, in1=xs[:, j:j + m, :], op0=ALU.max, op1=ALU.add)\
                    .then_inc(result_ready, 1)


def laid_out(x, src, dst, edge_attr_16, edge_attr_64, L0_gnn_W_edge, L0_gnn_b_edge, L0_gnn_W1, L0_gnn_b1,
             L0_gnn_gamma, L0_gnn_beta, L0_gnn_W2, L0_gnn_b2, L1_gnn_M_W, L1_gnn_M_b, L1_gnn_U_W, L1_gnn_U_b):
    def tiles(a, fill):
        padded = np.full(TILES * P, fill, np.int32)
        padded[:EDGES] = a
        return padded.reshape(TILES, P).T

    def features(a):
        padded = np.zeros((TILES * P, a.shape[1]), np.float32)
        padded[:EDGES] = a
        return np.ascontiguousarray(padded.reshape(BATCHES, BATCH * P, -1).transpose(0, 2, 1))

    params = np.zeros((P, PARAM_COLS), np.float32)

    def put(name, block):
        params[:block.shape[0], PARAMS[name]] = block

    def twice(w):
        both = np.zeros((2 * D, 2 * D), np.float32)
        both[:D, :D] = both[D:, D:] = w
        return both

    put("identity", np.eye(P, dtype=np.float32))
    put("iota", np.tile(np.arange(WINDOW, dtype=np.float32), (P, 1)))
    put("ones", np.ones((1, P), np.float32))
    put("eps", np.full((P, 1), LN_EPS, np.float32))
    put("w_edge", L0_gnn_W_edge.T)
    put("b_edge", np.tile(L0_gnn_b_edge, (P, 1)))
    put("w1_twice", twice(L0_gnn_W1.T))
    put("w2_twice", twice(L0_gnn_W2.T))
    put("b2", np.tile(L0_gnn_b2, (P, 1)))
    put("m_node_twice", twice(L1_gnn_M_W[:, :D].T))
    put("m_b", np.tile(L1_gnn_M_b, (P, 1)))
    put("m_edge", L1_gnn_M_W[:, D:].T)
    put("u_node_twice", twice(L1_gnn_U_W[:, :D].T))
    put("u_b", np.tile(L1_gnn_U_b, 2)[:, None])
    put("u_sum", L1_gnn_U_W[:, D:].T)
    put("b1", np.tile(L0_gnn_b1, 2)[:, None])
    put("gamma", L0_gnn_gamma[:, None])
    put("beta", L0_gnn_beta[:, None])
    idx = tiles(src, 0)
    return {
        "x": np.ascontiguousarray(x).reshape(NODE_P, NODE_COLS, D),
        "idx": np.ascontiguousarray(np.concatenate([idx, idx[:, :2 * BATCH]], axis=1)),
        "dst": np.ascontiguousarray(tiles(dst, N)),
        "attr0": features(edge_attr_16),
        "attr1": features(edge_attr_64),
        "params": params,
    }


def kernel(**inputs):
    import concourse.bacc as bacc
    from concourse.bass_utils import run_bass_kernel_spmd

    arrays = laid_out(**{name: np.asarray(a) for name, a in inputs.items()})
    nc = bacc.Bacc("TRN2", target_bir_lowering=False, num_devices=1)
    ins = [nc.dram_tensor(name, a.shape, mybir.dt.from_np(a.dtype), kind="ExternalInput").ap()
           for name, a in arrays.items()]
    out = nc.dram_tensor("out", (NODE_P, NODE_COLS, D), F32, kind="ExternalOutput").ap()
    build(nc, *ins, out)
    result = run_bass_kernel_spmd(nc, [arrays], core_ids=[0])
    return result.results[0]["out"].reshape(N, D)
```
